# Optimizing a Trainium2 kernel written in Bass

```python
import numpy as np
import jax
import jax.numpy as jnp

def _softmax(x, axis=-1):
    return jax.nn.softmax(x, axis=axis)

def _gelu(x):
    return jax.nn.gelu(x, approximate=True)

def _silu(x):
    return jax.nn.silu(x)

def _sigmoid(x):
    return jax.nn.sigmoid(x)

def _layernorm(x, axis=-1, eps=1e-05):
    m = jnp.mean(x, axis=axis, keepdims=True)
    v = jnp.var(x, axis=axis, keepdims=True)
    return (x - m) / jnp.sqrt(v + eps)

def _scatter_add(tgt, idx, src, axis=0):
    return tgt.at[idx].add(src)

def _segment_sum(src, seg, n):
    return jax.ops.segment_sum(src, seg, n)
kernel_name = 'mk_gnn_preln_d2_gnn_r8_ed1fe4'

def setup_inputs(seed: int=0):
    np.random.seed(seed)
    _w = jnp.asarray

    def _rec_inputs():
        import jax
        import jax.numpy as jnp
        _gk = jax.random.key(seed)
        x = -0.0003713 + 1 * jax.random.normal(jax.random.fold_in(_gk, 1), (12500, 128), jnp.float32)
        src = jax.random.randint(jax.random.fold_in(_gk, 2), (400000,), 0, 12500, jnp.int32)
        dst = jnp.minimum((12500 * jax.random.uniform(jax.random.fold_in(_gk, 3), (400000,)) ** 2.0).astype(jnp.int32), 99999)
        _o = jnp.argsort(dst, stable=True)
        src = src[_o]
        dst = dst[_o]
        edge_type_16 = jax.random.randint(jax.random.fold_in(_gk, 12), (400000,), 0, 16, jnp.int32)
        return (x, src, dst, edge_type_16)
    x, src, dst, edge_type_16 = _rec_inputs()

    def _L0_gnn_setup():
        import jax, jax.numpy as jnp
        import numpy as np
        N_NODES = 12500
        HIDDEN = 128
        N_EDGES = 75000

        def _sage_conv(x, src, dst, W_l, W_r, b, num_nodes):
            msgs = x[src]
            agg = jax.ops.segment_sum(msgs, dst, num_segments=num_nodes)
            cnt = jax.ops.segment_sum(jnp.ones((src.shape[0], 1), dtype=x.dtype), dst, num_segments=num_nodes)
            mean = agg / jnp.maximum(cnt, 1.0)
            return mean @ W_l.T + x @ W_r.T + b
        key = jax.random.key(seed)
        ks = jax.random.split(key, 8)
        scale = 1.0 / np.sqrt(HIDDEN)
        x = jax.random.normal(ks[0], (N_NODES, HIDDEN), dtype=jnp.float32)
        edge_index = jax.random.randint(ks[1], (2, N_EDGES), 0, N_NODES, dtype=jnp.int64)
        W1_l = jax.random.normal(ks[2], (HIDDEN, HIDDEN), dtype=jnp.float32) * scale
        W1_r = jax.random.normal(ks[3], (HIDDEN, HIDDEN), dtype=jnp.float32) * scale
        b1 = jnp.zeros((HIDDEN,), dtype=jnp.float32)
        W2_l = jax.random.normal(ks[4], (HIDDEN, HIDDEN), dtype=jnp.float32) * scale
        W2_r = jax.random.normal(ks[5], (HIDDEN, HIDDEN), dtype=jnp.float32) * scale
        b2 = jnp.zeros((HIDDEN,), dtype=jnp.float32)
        return {'x': x, 'edge_index': edge_index, 'W1_l': W1_l, 'W1_r': W1_r, 'b1': b1, 'W2_l': W2_l, 'W2_r': W2_r, 'b2': b2}
    _L0_gnn_all = _L0_gnn_setup()
    _L0_gnn_in = {k: v for k, v in _L0_gnn_all.items() if k in ('W1_l', 'W1_r', 'b1', 'W2_l', 'W2_r', 'b2')}
    del _L0_gnn_all

    def _L1_gnn_setup():
        import jax, jax.numpy as jnp
        import numpy as np
        NUM_NODES = 12500
        NUM_EDGES = 80000
        IN_DIM = 128
        OUT_DIM = 128
        NUM_REL = 16
        key = jax.random.key(seed)
        k1, k2, k3, k4, k5 = jax.random.split(key, 5)
        x = jax.random.normal(k1, (NUM_NODES, IN_DIM), dtype=jnp.float32)
        edge_index = jax.random.randint(k2, (2, NUM_EDGES), 0, NUM_NODES, dtype=jnp.int64)
        edge_types = jax.random.randint(k3, (NUM_EDGES,), 0, NUM_REL, dtype=jnp.int64)
        rw_bound = float(np.sqrt(6.0 / (IN_DIM * OUT_DIM + NUM_REL)))
        relation_weights = jax.random.uniform(k4, (NUM_REL, IN_DIM, OUT_DIM), dtype=jnp.float32, minval=-rw_bound, maxval=rw_bound)
        sw_bound = float(np.sqrt(6.0 / (IN_DIM + OUT_DIM)))
        self_weight = jax.random.uniform(k5, (IN_DIM, OUT_DIM), dtype=jnp.float32, minval=-sw_bound, maxval=sw_bound)
        bias = jnp.zeros((OUT_DIM,), dtype=jnp.float32)
        return {'x': x, 'edge_index': edge_index, 'edge_types': edge_types, 'relation_weights': relation_weights, 'self_weight': self_weight, 'bias': bias}
    _L1_gnn_all = _L1_gnn_setup()
    _L1_gnn_in = {k: v for k, v in _L1_gnn_all.items() if k in ('relation_weights', 'self_weight', 'bias')}
    del _L1_gnn_all
    return {'x': x, 'src': src, 'dst': dst, 'edge_type_16': edge_type_16, 'L0_gnn_W1_l': _L0_gnn_in['W1_l'], 'L0_gnn_W1_r': _L0_gnn_in['W1_r'], 'L0_gnn_b1': _L0_gnn_in['b1'], 'L0_gnn_W2_l': _L0_gnn_in['W2_l'], 'L0_gnn_W2_r': _L0_gnn_in['W2_r'], 'L0_gnn_b2': _L0_gnn_in['b2'], 'L1_gnn_relation_weights': _L1_gnn_in['relation_weights'], 'L1_gnn_self_weight': _L1_gnn_in['self_weight'], 'L1_gnn_bias': _L1_gnn_in['bias']}

def reference(x, src, dst, edge_type_16, L0_gnn_W1_l, L0_gnn_W1_r, L0_gnn_b1, L0_gnn_W2_l, L0_gnn_W2_r, L0_gnn_b2, L1_gnn_relation_weights, L1_gnn_self_weight, L1_gnn_bias):
    import jax
    import jax.numpy as jnp

    def _L0_gnn_ref(x, edge_index, W1_l, W1_r, b1, W2_l, W2_r, b2):
        import jax, jax.numpy as jnp
        import numpy as np
        N_NODES = 12500
        HIDDEN = 128
        N_EDGES = 75000

        def _sage_conv(x, src, dst, W_l, W_r, b, num_nodes):
            msgs = x[src]
            agg = jax.ops.segment_sum(msgs, dst, num_segments=num_nodes)
            cnt = jax.ops.segment_sum(jnp.ones((src.shape[0], 1), dtype=x.dtype), dst, num_segments=num_nodes)
            mean = agg / jnp.maximum(cnt, 1.0)
            return mean @ W_l.T + x @ W_r.T + b
        src, dst = (edge_index[0], edge_index[1])
        n = x.shape[0]
        h = _sage_conv(x, src, dst, W1_l, W1_r, b1, n)
        h = jax.nn.relu(h)
        out = _sage_conv(h, src, dst, W2_l, W2_r, b2, n)
        return out

    def _L1_gnn_ref(x, edge_index, edge_types, relation_weights, self_weight, bias):
        import jax, jax.numpy as jnp
        import numpy as np
        NUM_NODES = 12500
        NUM_EDGES = 80000
        IN_DIM = 128
        OUT_DIM = 128
        NUM_REL = 16
        num_nodes = x.shape[0]
        self_msg = x @ self_weight
        transformed = jnp.einsum('ni,rio->rno', x, relation_weights)
        src = edge_index[0]
        dst = edge_index[1]
        msgs = transformed[edge_types, src]
        neighbor_msg = jax.ops.segment_sum(msgs, dst, num_segments=num_nodes)
        return jax.nn.relu(self_msg + neighbor_msg + bias)
    edge_index = jnp.stack([src, dst])
    h = jnp.maximum(_layernorm(x, axis=-1), 0.0)
    x = x + _L0_gnn_ref(h, edge_index, L0_gnn_W1_l, L0_gnn_W1_r, L0_gnn_b1, L0_gnn_W2_l, L0_gnn_W2_r, L0_gnn_b2)
    h = jnp.maximum(_layernorm(x, axis=-1), 0.0)
    x = x + _L1_gnn_ref(h, edge_index, edge_type_16, L1_gnn_relation_weights, L1_gnn_self_weight, L1_gnn_bias)
    return x

_drawn_inputs = setup_inputs


def setup_inputs(seed=0):
    import zlib

    import numpy as np

    out = dict(_drawn_inputs(seed))
    spreads = {'L0_gnn_b1': (0.0, 0.1), 'L0_gnn_b2': (0.0, 0.1), 'L1_gnn_bias': (0.0, 0.1)}
    factors = {}
    for name, (base, spread) in spreads.items():
        noise = np.random.default_rng([zlib.crc32(name.encode()), seed]).standard_normal(out[name].shape)
        drawn = base * np.exp(spread * noise) if base else spread * noise
        out[name] = jnp.asarray(drawn.astype(out[name].dtype))
    for name, factor in factors.items():
        out[name] = (out[name] * factor).astype(out[name].dtype)
    return out
```

```python
from contextlib import ExitStack

import concourse.bass as bass
from concourse import mybir

ALU = mybir.AluOpType
ACT = mybir.ActivationFunctionType
AX = mybir.AxisListType
DVE = mybir.EngineType.DVE
F32 = mybir.dt.float32
BF16 = mybir.dt.bfloat16
I32 = mybir.dt.int32

P = 128
WIN = 32
BANK = 512
EPS = 1e-5


def chunks_per_group(n_chunks):
    return max(k for k in (25, 20, 15, 10, 5) if n_chunks % k == 0)


def gnn_kernel(nc, x, src, dst, edge_type, w1l, w1r, b1, w2l, w2r, b2, w_rel, w_self, bias, out):
    N = x.shape[0]
    C = src.shape[1]
    K = chunks_per_group(C)
    G = C // K
    HALF = [(0, K // 2), (K // 2, K)]
    NPS = 5
    CNT = 5
    NR = w_rel.shape[0] // P
    RB = NR * P // BANK
    T = 2 * -(-N // (2 * P))
    FULL = N // P
    REST = N - FULL * P

    table = nc.dram_tensor("table", (T * P, P), F32, kind="Internal").ap()
    table2 = nc.dram_tensor("table2", (T * P, P), F32, kind="Internal").ap()
    table_rel = nc.dram_tensor("table_rel", (T * P * NR, P), F32, kind="Internal").ap()
    rel_index = nc.dram_tensor("rel_index", (P, C), I32, kind="Internal").ap()
    table_rel_blocks = table_rel.rearrange("(t p r) f -> t p (r f)", p=P, r=NR)

    ctx = ExitStack()
    with ctx:
        def sb(name, shape, dt):
            return ctx.enter_context(nc.sbuf_tensor(name, shape, dt))

        def sem(name):
            return ctx.enter_context(nc.semaphore(name))

        xs = sb("xs", [P, T * P], F32)
        self_term = sb("self_term", [P, T * P], F32)
        acc = sb("acc", [P, T * P + WIN], F32)
        rows = sb("rows", [P, K * P], F32)
        onehot = sb("onehot", [P, K, WIN], F32)
        dst_i = sb("dst_i", [P, C], I32)
        dst_rel = sb("dst_rel", [P, C], BF16)
        index = sb("index", [P, K], I32)
        iota = sb("iota", [P, P], F32)
        iota_b = sb("iota_b", [P, P], BF16)
        ident = sb("ident", [P, P], F32)
        W1l, W1r, W2l, W2r, Wself = (sb(n, [P, P], F32) for n in ("W1l", "W1r", "W2l", "W2r", "Wself"))
        Wrel = sb("Wrel", [P, NR * P], F32)
        bias_rows = sb("bias_rows", [1, 3 * P], F32)
        ones_row = sb("ones_row", [1, P], F32)
        zero_b = sb("zero_b", [P, P], BF16)
        mean_var = sb("mean_var", [P, T, 2], F32)
        stats = sb("stats", [P, 2, 6], F32)
        moments_pair = sb("moments_pair", [P, 2, 2], F32)
        rstd = sb("rstd", [P, T], F32)
        shift = sb("shift", [P, T], F32)
        rcount = sb("rcount", [P, T], F32)
        acc_block = [sb(f"acc_block{u}", [P, P], F32) for u in range(2)]
        pre = [sb(f"pre{u}", [P, P], F32) for u in range(2)]
        h = [sb(f"h{u}", [P, P], F32) for u in range(2)]
        hT = [sb(f"hT{u}", [P, P], F32) for u in range(2)]
        dst_hi_i = sb("dst_hi_i", [P, K], I32)
        dst_lo_i = sb("dst_lo_i", [P, K], I32)
        CC = 5
        dst_hi = sb("dst_hi", [P, K], BF16)
        dst_lo = sb("dst_lo", [P, K], BF16)
        hot_hi = sb("hot_hi", [P, CC, T], BF16)
        hot_lo = sb("hot_lo", [P, CC, P], BF16)
        dst_cur = sb("dst_cur", [P, 1], F32)
        reach = sb("reach", [P, 4], F32)
        far_row = sb("far_row", [1, 1], F32)
        spare = sb("spare", [P, 16], F32)
        far = sb("far", [1, 1], I32)

        hot_block = onehot[:, :, :].rearrange("p k w -> p (k w)")[:, 0:P]
        base_all = acc[:, 0:C].bitcast(I32)
        src_all = acc[:, C:2 * C].bitcast(I32)
        type_all = acc[:, 2 * C:3 * C].bitcast(I32)
        rel_f = self_term[:, 0:C]
        rel_out = rows[:, 0:NR * P]

        ps = [ctx.enter_context(nc.psum_tensor(f"ps{i}", [P, BANK], F32)) for i in range(8)]

        s_x = sem("s_x")
        s_dst = sem("s_dst")
        s_setup_in = sem("s_setup_in")
        s_w = sem("s_w")
        s_const = sem("s_const")
        s_ident = sem("s_ident")
        s_v = sem("s_v")
        s_reach = sem("s_reach")
        s_reach_t = sem("s_reach_t")
        s_far = sem("s_far")
        s_ri = sem("s_ri")
        s_ri_out = sem("s_ri_out")
        s_stat = sem("s_stat")
        s_moments = sem("s_moments")
        s_std = sem("s_std")
        s_norm = sem("s_norm")
        s_zero = sem("s_zero")
        s_ab = sem("s_ab")
        s_pp = sem("s_pp")
        s_pre = sem("s_pre")
        s_h = sem("s_h")
        s_hst = [sem(f"s_hst{u}") for u in range(2)]
        s_tp = sem("s_tp")
        s_hT = sem("s_hT")
        s_y = sem("s_y")
        s_yd = sem("s_yd")
        s_z = sem("s_z")
        s_zc = sem("s_zc")
        s_zst = [sem(f"s_zst{r}") for r in range(RB)]
        s_out = [sem(f"s_out{u}") for u in range(2)]
        s_agg = [sem(f"s_agg{n}") for n in range(3)]
        s_idx = [sem(f"s_idx{i}") for i in range(2)]
        s_row = [sem(f"s_row{j}") for j in range(K)]
        s_mm = [sem(f"s_mm{j}") for j in range(K)]
        s_add = [sem(f"s_add{j}") for j in range(K)]
        s_hot = [sem(f"s_hot{i}") for i in range(2)]
        s_hl = sem("s_hl")
        s_ch = sem("s_ch")
        s_cm = sem("s_cm")
        s_cnt = sem("s_cnt")
        g_idx = sem("g_idx")
        g_row = sem("g_row")
        g_hot = sem("g_hot")
        g_mm = sem("g_mm")
        g_add = sem("g_add")
        g_own = sem("g_own")
        g_free = sem("g_free")

        s_apart = {e: sem(f"s_apart_{e}") for e in ("sp", "pool", "dve")}

        block = ctx.enter_context(nc.Block())
        STAGE_A, STAGE_B, STAGE_C, STAGE_D = range(4)


        def index_source(layer):
            return rel_index if layer == 2 else src

        def gather_table(layer):
            return (table, table2, table_rel)[layer]

        @block.sync
        def _(eng):
            eng.dma_start(xs[:, 0:FULL * P].rearrange("p (t f) -> p t f", f=P),
                          x[0:FULL * P, :].rearrange("(t p) f -> p t f", p=P)).then_inc(s_x, 16)
            if REST:
                eng.wait_ge(s_const, 1)
                eng.dma_start(xs[0:REST, FULL * P:(FULL + 1) * P], x[FULL * P:N, :]).then_inc(s_x, 16)
            for k, s in enumerate([*s_hst, *s_zst, *s_out]):
                eng.dma_start(spare[k:k + 1, :], b1[:, 0:16]).then_inc(s, 16)
            eng.wait_ge(s_ri, 1)
            eng.dma_start(rel_index, rel_f.bitcast(I32)).then_inc(s_ri_out, 16)

            def store_h(n, tab):
                with eng.Fori(0, T // 2) as i:
                    for u in range(2):
                        row = eng.snap((i * 2 + u) * P)
                        eng.wait_ge(s_h, eng.snap(i * 2 + (n * T + u + 1)))
                        eng.sem_inc(s_apart["sp"], 1)
                        eng.dma_start(tab[bass.ds(row, P), :], h[u][:, :]).then_inc(s_hst[u], 16)

            def store_relations():
                with eng.Fori(0, T) as t:
                    for r in range(RB):
                        part = slice(r * BANK, (r + 1) * BANK)
                        eng.wait_ge(s_zc, eng.snap(t * RB + (RB + r + 1)))
                        eng.sem_inc(s_apart["sp"], 1)
                        eng.dma_start(table_rel_blocks[bass.ds(t, 1), :, part].rearrange("t p f -> (t p) f"),
                                      rel_out[:, part]).then_inc(s_zst[r], 16)

            def feed_indices(layer):
                source = index_source(layer)

                def fast():
                    with eng.Fori(0, G) as g:
                        now = eng.snap(g + (layer * G + 1))
                        for i, (a, b) in enumerate(HALF):
                            eng.wait_ge(s_mm[b - 1], now)
                            eng.sem_inc(s_apart["sp"], 1)
                            eng.dma_start(index[:, a:b], source[:, bass.ds(g * K + a, b - a)]).then_inc(s_idx[i], 16)

                def general():
                    with eng.Fori(0, C) as c:
                        eng.wait_ge(g_free, eng.snap(c + (layer * C + 1)))
                        eng.sem_inc(s_apart["sp"], 1)
                        eng.dma_start(index[:, 0:1], source[:, bass.ds(c, 1)],
                                      allow_slow_non_contiguous=True).then_inc(g_idx, 16)

                with eng.If(is_far == 0):
                    fast()
                with eng.Else():
                    general()

            eng.wait_ge(s_far, 1)
            is_far = eng.value_load(far[0:1, 0:1])
            store_h(0, table)
            feed_indices(0)
            store_h(1, table2)
            feed_indices(1)
            eng.wait_ge(s_ri_out, 16)
            store_relations()
            feed_indices(2)
            with eng.Fori(0, FULL // 2) as i:
                for u in range(2):
                    row = eng.snap((i * 2 + u) * P)
                    eng.wait_ge(s_h, eng.snap(i * 2 + (3 * T + u + 1)))
                    eng.sem_inc(s_apart["sp"], 1)
                    eng.dma_start(out[bass.ds(row, P), :], h[u][:, :]).then_inc(s_out[u], 16)
            stores = [FULL // 2, FULL // 2]
            for t in range(FULL // 2 * 2, T):
                n = P if t < FULL else (REST if t == FULL else 0)
                if n:
                    eng.wait_ge(s_h, 3 * T + t + 1)
                    eng.dma_start(out[t * P:t * P + n, :], h[t % 2][0:n, :]).then_inc(s_out[t % 2], 16)
                    stores[t % 2] += 1
            for u in range(2):
                eng.wait_ge(s_out[u], 16 * stores[u] + 16)

        @block.gpsimd
        def _(eng):
            eng.memset(xs[:, FULL * P:T * P], 0.0).then_inc(s_const, 1)
            eng.iota(iota[:, :], [[1, P]], base=0, channel_multiplier=0,
                     allow_small_or_imprecise_dtypes=True).then_inc(s_const, 1)
            eng.iota(iota_b[:, :], [[1, P]], base=0, channel_multiplier=0,
                     allow_small_or_imprecise_dtypes=True).then_inc(s_const, 1)
            eng.memset(ident[:, :], 1.0).then_inc(s_ident, 1)
            eng.wait_ge(s_ident, 1)
            eng.affine_select(ident[:, :], ident[:, :], [[1, P]], ALU.is_equal, 0.0, base=0,
                              channel_multiplier=-1).then_inc(s_const, 1)
            eng.memset(ones_row[:, :], 1.0).then_inc(s_const, 1)
            eng.memset(zero_b[:, :], 0.0).then_inc(s_const, 1)
            eng.wait_ge(s_far, 1)
            is_far = eng.value_load(far[0:1, 0:1])

            def gather(layer):
                tab = gather_table(layer)
                stored, filled = (s_hst, 16 * (T // 2) * (layer + 1) + 16) if layer < 2 else (s_zst, 16 * T + 16)
                for s in stored:
                    eng.wait_ge(s, filled)

                def fast():
                    with eng.Fori(0, G) as g:
                        now = eng.snap(g + (layer * G + 1))
                        landed = eng.snap((g + (layer * G + 1)) * 16)
                        for i, (a, b) in enumerate(HALF):
                            eng.wait_ge(s_idx[i], landed)
                            for j in range(a, b):
                                eng.wait_ge(s_mm[j], now)
                                eng.sem_inc(s_apart["pool"], 1)
                                eng.indirect_dma_start(
                                    rows[:, j * P:(j + 1) * P], None, tab,
                                    bass.IndirectOffsetOnAxis(index[:, j:j + 1], 0)).then_inc(s_row[j], 16)

                def general():
                    with eng.Fori(0, C) as c:
                        eng.wait_ge(g_idx, eng.snap((c + (layer * C + 1)) * 16))
                        eng.sem_inc(s_apart["pool"], 1)
                        eng.indirect_dma_start(
                            rows[:, 0:P], None, tab,
                            bass.IndirectOffsetOnAxis(index[:, 0:1], 0)).then_inc(g_row, 16)

                with eng.If(is_far == 0):
                    fast()
                with eng.Else():
                    general()

            for layer in range(3):
                gather(layer)

        @block.tensor
        def _(eng):
            for s in [*s_mm, s_cm, g_mm, g_free]:
                eng.sem_inc(s, 1)
            for s in (s_pp, s_tp, s_y):
                eng.sem_inc(s, 2)
            eng.sem_inc(s_z, 2 * RB)
            eng.wait_ge(s_const, 6)
            eng.wait_ge(s_reach, 1)
            eng.matmul(ps[7][0:1, 0:P], reach[:, 2:3], ident[:, :], start=True, stop=True).then_inc(s_reach_t, 1)
            eng.wait_ge(s_w, 16 * 9)
            eng.wait_ge(s_far, 1)
            is_far = eng.value_load(far[0:1, 0:1])

            def neighbour_product(n, i, u, weight):
                eng.wait_ge(s_ab, eng.snap(i * 2 + (n * T + u + 1)))
                eng.wait_ge(s_pre, eng.snap(i * 2 + (n * T + u + 1)))
                eng.matmul(ps[4 + u][:, 0:P], acc_block[u][:, :], weight, start=True, stop=True).then_inc(s_pp, 1)

            def self_product(n, i, u, weight):
                b = bias_rows[:, n * P:(n + 1) * P]
                eng.wait_ge(s_h, eng.snap(i * 2 + (n * T + u + 1)))
                eng.transpose(ps[u][:, 0:P], h[u][:, :], ident[:, :]).then_inc(s_tp, 1)
                eng.wait_ge(s_yd, eng.snap(i * 2 + (n * T + u + 1)))
                eng.wait_ge(s_hT, eng.snap(i * 2 + (n * T + u + 1)))
                eng.matmul(ps[2 + u][:, 0:P], ones_row[:, :], b, start=True, stop=False)
                eng.matmul(ps[2 + u][:, 0:P], hT[u][:, :], weight, start=False, stop=True).then_inc(s_y, 1)

            def relation_products(i, u):
                for r in range(RB):
                    eng.wait_ge(s_zc, eng.snap(i * (2 * RB) + (u * RB + r + 1)))
                    eng.matmul(ps[4 + r][:, :], hT[u][:, :], Wrel[:, r * BANK:(r + 1) * BANK],
                               start=True, stop=True).then_inc(s_z, 1)

            def aggregate(layer):
                def fast():
                    with eng.Fori(0, G) as g:
                        now = eng.snap(g + (layer * G + 1))
                        after = eng.snap(g + (layer * G + 2))
                        landed = eng.snap((g + (layer * G + 1)) * 16)
                        for i, (a, b) in enumerate(HALF):
                            eng.wait_ge(s_hot[i], now)
                            for j in range(a, b):
                                eng.wait_ge(s_row[j], landed)
                                if j >= NPS:
                                    eng.wait_ge(s_add[j - NPS], after)
                                else:
                                    eng.wait_ge(s_add[j - NPS + K], now)
                                eng.matmul(ps[j % NPS][:, 0:WIN], rows[:, j * P:(j + 1) * P], onehot[:, j, :],
                                           start=True, stop=True).then_inc(s_mm[j], 1)
                        if layer == 0:
                            count_group(g)

                def general():
                    with eng.Fori(0, C) as c:
                        landed = eng.snap((c + (layer * C + 1)) * 16)
                        with eng.Fori(0, T) as t:
                            n = eng.snap((c + layer * C) * T + t + 1)
                            eng.wait_ge(g_row, landed)
                            eng.wait_ge(g_hot, n)
                            eng.wait_ge(g_add, n)
                            eng.matmul(ps[0][:, 0:P], rows[:, 0:P], hot_block, start=True, stop=True).then_inc(g_mm, 1)
                        eng.wait_ge(g_mm, eng.snap((c + (layer * C + 1)) * T + 1))
                        eng.sem_inc(g_free, 1)
                    if layer == 0:
                        with eng.Fori(0, G) as g:
                            count_group(g)

                def count_group(g):
                    for q in range(K // CC):
                        eng.wait_ge(s_ch, eng.snap(g * (2 * (K // CC)) + 2 * (q + 1)))
                        for j in range(CC):
                            mm = eng.matmul(ps[CNT][:, 0:T], hot_lo[:, j, :], hot_hi[:, j, :],
                                            start=False, stop=False, skip_group_check=True)
                        mm.then_inc(s_cm, 1)

                eng.wait_ge(s_yd, (layer + 1) * T + 2)
                eng.wait_ge(s_pre, layer * T + 2)
                if layer == 2:
                    eng.wait_ge(s_zc, RB * T + RB)
                if layer == 0:
                    eng.matmul(ps[CNT][:, 0:T], zero_b[:, :], zero_b[:, 0:T], start=True, stop=False,
                               skip_group_check=True)
                with eng.If(is_far == 0):
                    fast()
                with eng.Else():
                    general()
                if layer == 0:
                    eng.matmul(ps[CNT][:, 0:T], zero_b[:, :], zero_b[:, 0:T], start=False, stop=True,
                               skip_group_check=True).then_inc(s_cnt, 1)

            with eng.Fori(0, T // 2) as i:
                for u in range(2):
                    self_product(0, i, u, W1r[:, :])
            aggregate(0)
            with eng.Fori(0, T // 2) as i:
                for u in range(2):
                    neighbour_product(0, i, u, W1l[:, :])
                for u in range(2):
                    self_product(1, i, u, W2r[:, :])
            aggregate(1)
            with eng.Fori(0, T // 2) as i:
                for u in range(2):
                    neighbour_product(1, i, u, W2l[:, :])
            eng.wait_ge(s_pre, 2 * T + 2)
            with eng.Fori(0, T // 2) as i:
                for u in range(2):
                    self_product(2, i, u, Wself[:, :])
                    relation_products(i, u)
            aggregate(2)
            with eng.Fori(0, T // 2) as i:
                for u in range(2):
                    neighbour_product(2, i, u, ident[:, :])

        @block.scalar
        def _(eng):
            eng.dma_start(dst_i[:, :], dst).then_inc(s_dst, 16)
            eng.dma_start(base_all, dst[0:1, :].broadcast_to([P, C])).then_inc(s_setup_in, 16)
            eng.dma_start(src_all, src).then_inc(s_setup_in, 16)
            eng.dma_start(type_all, edge_type).then_inc(s_setup_in, 16)
            for w, a in ((W1l, w1l), (W1r, w1r), (W2l, w2l), (W2r, w2r), (Wself, w_self)):
                eng.dma_start(w[:, :], a).then_inc(s_w, 16)
            eng.dma_start(Wrel[:, :].rearrange("k (r n) -> k r n", n=P),
                          w_rel.rearrange("(r k) n -> k r n", k=P)).then_inc(s_w, 16)
            for n, a in enumerate((b1, b2, bias)):
                eng.dma_start(bias_rows[:, n * P:(n + 1) * P], a).then_inc(s_w, 16)
            eng.sem_inc(s_zc, RB)

            def std(n):
                eng.wait_ge(s_moments, n + 1)
                eng.activation(rstd[:, :], mean_var[:, :, 1], ACT.Sqrt).then_inc(s_std, 1)

            def copy_acc(n, i, u):
                eng.wait_ge(s_pp, eng.snap(i * 2 + (n * T + u + 1)))
                eng.activation(acc_block[u][:, :], acc[:, bass.ds((i * 2 + u) * P, P)], ACT.Copy).then_inc(s_ab, 1)

            def h_free(n, i, u):
                if n < 2:
                    eng.wait_ge(s_hst[u], eng.snap((i + (n * (T // 2) + 1)) * 16))
                else:
                    eng.wait_ge(s_hst[u], 16 * T + 16)
                eng.wait_ge(s_tp, eng.snap(i * 2 + (n * T + u + 1)))

            def norm_h(n, i, u):
                t = i * 2 + u
                h_free(n, i, u)
                eng.activation(h[u][:, :], xs[:, bass.ds(t * P, P)], ACT.Relu, bias=shift[:, bass.ds(t, 1)],
                               scale=rstd[:, bass.ds(t, 1)]).then_inc(s_h, 1)

            def copy_hT(n, i, u):
                eng.wait_ge(s_tp, eng.snap(i * 2 + (n * T + u + 3)))
                eng.wait_ge(s_y, eng.snap(i * 2 + (n * T + u + 1)))
                if n == 2:
                    eng.wait_ge(s_z, eng.snap(i * (2 * RB) + (u + 1) * RB))
                eng.activation(hT[u][:, :], ps[u][:, 0:P], ACT.Copy).then_inc(s_hT, 1)

            std(0)
            eng.wait_ge(s_norm, 1)
            with eng.Fori(0, T // 2) as i:
                for u in range(2):
                    norm_h(0, i, u)
                for u in range(2):
                    copy_hT(0, i, u)
            eng.wait_ge(s_agg[0], 1)
            with eng.Fori(0, T // 2) as i:
                for u in range(2):
                    copy_acc(0, i, u)
                for u in range(2):
                    h_free(1, i, u)
                    eng.wait_ge(s_pre, eng.snap(i * 2 + (2 + u + 1)))
                    eng.activation(h[u][:, :], pre[u][:, :], ACT.Relu).then_inc(s_h, 1)
                for u in range(2):
                    copy_hT(1, i, u)
            eng.wait_ge(s_agg[1], 1)
            with eng.Fori(0, T // 2) as i:
                for u in range(2):
                    copy_acc(1, i, u)
            std(1)
            eng.wait_ge(s_norm, 2)
            with eng.Fori(0, T // 2) as i:
                for u in range(2):
                    norm_h(2, i, u)
                for u in range(2):
                    copy_hT(2, i, u)
                    for r in range(RB):
                        eng.wait_ge(s_z, eng.snap(i * (2 * RB) + (2 * RB + u * RB + r + 1)))
                        eng.wait_ge(s_zst[r], eng.snap((i * 2 + (u + 1)) * 16))
                        eng.activation(rel_out[:, r * BANK:(r + 1) * BANK], ps[4 + r][:, :],
                                       ACT.Copy).then_inc(s_zc, 1)
            eng.wait_ge(s_agg[2], 1)
            with eng.Fori(0, T // 2) as i:
                for u in range(2):
                    copy_acc(2, i, u)

        @block.vector
        def _(eng):
            for s in [*s_add, g_add]:
                eng.sem_inc(s, 1)
            for s in (s_yd, s_pre):
                eng.sem_inc(s, 2)
            eng.wait_ge(s_dst, 16)
            eng.wait_ge(s_setup_in, 48)
            eng.tensor_tensor(rel_f, dst_i[:, :], base_all, ALU.subtract).then_inc(s_v, 1)
            eng.wait_ge(s_v, 1)
            eng.tensor_copy(dst_rel[:, :], rel_f).then_inc(s_v, 1)
            eng.tensor_reduce(reach[:, 0:1], rel_f, AX.X, ALU.max).then_inc(s_v, 1)
            eng.tensor_reduce(reach[:, 1:2], rel_f, AX.X, ALU.min).then_inc(s_v, 1)
            eng.wait_ge(s_v, 4)
            eng.tensor_scalar(reach[:, 3:4], reach[:, 0:1], float(WIN - 1), None, ALU.subtract).then_inc(s_v, 1)
            eng.wait_ge(s_v, 5)
            eng.scalar_tensor_tensor(out=reach[:, 2:3], in0=reach[:, 1:2], scalar=-1.0, in1=reach[:, 3:4],
                                     op0=ALU.mult, op1=ALU.max).then_inc(s_reach, 1)
            eng.wait_ge(s_reach_t, 1)
            eng.tensor_reduce(far_row[:, :], ps[7][0:1, 0:P], AX.X, ALU.max).then_inc(s_v, 1)
            eng.wait_ge(s_v, 6)
            eng.tensor_scalar(far[:, :], far_row[:, :], 0.0, None, ALU.max).then_inc(s_far, 1)
            eng.scalar_tensor_tensor(out=rel_f.bitcast(I32), in0=src_all, scalar=float(NR), in1=type_all,
                                     op0=ALU.mult, op1=ALU.add).then_inc(s_ri, 1)
            eng.wait_ge(s_far, 1)
            is_far = eng.value_load(far[0:1, 0:1])

            def block_moments(n, t, u):
                eng.bn_stats(stats[:, u, :], xs[:, bass.ds(t * P, P)]).then_inc(s_stat, 1)


            def moments(n):
                with eng.Fori(0, T // 2) as i:
                    for u in range(2):
                        block_moments(n, i * 2 + u, u)
                    done = n * 5 * (T // 2)
                    eng.wait_ge(s_stat, eng.snap(i * 5 + (done + 2)))
                    eng.sem_inc(s_apart["dve"], 1)
                    for u in range(2):
                        eng.bn_aggr(moments_pair[:, u, :], stats[:, u, :]).then_inc(s_stat, 1)
                    eng.wait_ge(s_stat, eng.snap(i * 5 + (done + 4)))
                    eng.tensor_copy(mean_var[:, bass.ds(i * 2, 2), :], moments_pair[:, :, :]).then_inc(s_stat, 1)
                    eng.wait_ge(s_stat, eng.snap(i * 5 + (done + 5)))
                v = mean_var[:, :, 1]
                eng.tensor_scalar(v, v, EPS, None, ALU.add).then_inc(s_moments, 1)
                eng.wait_ge(s_std, n + 1)
                eng.reciprocal(rstd[:, :], rstd[:, :]).then_inc(s_v, 1)
                eng.wait_ge(s_v, (7, 10)[n])
                eng.scalar_tensor_tensor(out=shift[:, :], in0=mean_var[:, :, 0], scalar=-1.0, in1=rstd[:, :],
                                         op0=ALU.mult, op1=ALU.mult).then_inc(s_norm, 1)

            def keep_self(n, i, u):
                t = i * 2 + u
                eng.wait_ge(s_y, eng.snap(i * 2 + (n * T + 2 + u + 1)))
                y = ps[2 + u][:, 0:P]
                if n == 1:
                    xt = xs[:, bass.ds(t * P, P)]
                    eng.tensor_tensor(xt, y, xt, ALU.add).then_inc(s_yd, 1)
                else:
                    eng.tensor_copy(self_term[:, bass.ds(t * P, P)], y).then_inc(s_yd, 1)

            def count_group(g):
                d = dst_i[:, bass.ds(g * K, K)]
                eng.wait_ge(s_cm, eng.snap(g * (K // CC) + 1))
                eng.tensor_scalar(dst_hi_i[:, :], d, 7, None, ALU.logical_shift_right).then_inc(s_hl, 1)
                eng.tensor_scalar(dst_lo_i[:, :], d, P - 1, None, ALU.bitwise_and).then_inc(s_hl, 1)
                eng.wait_ge(s_hl, eng.snap(g * 4 + 2))
                eng.tensor_copy(dst_hi[:, :], dst_hi_i[:, :]).then_inc(s_hl, 1)
                eng.tensor_copy(dst_lo[:, :], dst_lo_i[:, :]).then_inc(s_hl, 1)
                eng.wait_ge(s_hl, eng.snap(g * 4 + 4))
                for q in range(K // CC):
                    eng.wait_ge(s_cm, eng.snap(g * (K // CC) + (q + 1)))
                    cols = slice(q * CC, (q + 1) * CC)
                    eng.tensor_tensor(hot_hi[:, :, :], iota_b[:, 0:T].unsqueeze(1).broadcast_to([P, CC, T]),
                                      dst_hi[:, cols].unsqueeze(2).broadcast_to([P, CC, T]),
                                      ALU.is_equal).then_inc(s_ch, 1)
                    eng.tensor_tensor(hot_lo[:, :, :], iota_b[:, :].unsqueeze(1).broadcast_to([P, CC, P]),
                                      dst_lo[:, cols].unsqueeze(2).broadcast_to([P, CC, P]),
                                      ALU.is_equal).then_inc(s_ch, 1)

            def aggregate(layer):
                def fast():
                    with eng.Fori(0, G) as g:
                        now = eng.snap(g + (layer * G + 1))
                        after = eng.snap(g + (layer * G + 2))
                        for i, (a, b) in enumerate(HALF):
                            eng.wait_ge(s_mm[b - 1], now)
                            eng.tensor_tensor(
                                onehot[:, a:b, :], iota[:, 0:WIN].unsqueeze(1).broadcast_to([P, b - a, WIN]),
                                dst_rel[:, bass.ds(g * K + a, b - a)].unsqueeze(2).broadcast_to([P, b - a, WIN]),
                                ALU.is_equal).then_inc(s_hot[i], 1)
                        _, base = nc.values_load_multi_w_load_instructions(
                            dst_i[0:1, bass.ds(g * K, K)], engines=(DVE,), min_val=0, max_val=N - 1)
                        for j in range(K):
                            eng.wait_ge(s_mm[j], after)
                            eng.wait_ge(s_add[j - 1], after if j else now)
                            window = acc[:, bass.ds(base[j], WIN)]
                            eng.tensor_tensor(window, ps[j % NPS][:, 0:WIN], window, ALU.add).then_inc(s_add[j], 1)
                        if layer == 0:
                            count_group(g)
                    eng.wait_ge(s_add[K - 1], (layer + 1) * G + 1)

                def general():
                    with eng.Fori(0, C) as c:
                        eng.wait_ge(g_mm, eng.snap((c + layer * C) * T + 1))
                        eng.tensor_copy(dst_cur[:, :], dst_i[:, bass.ds(c, 1)]).then_inc(g_own, 1)
                        with eng.Fori(0, T) as t:
                            n = eng.snap((c + layer * C) * T + t + 1)
                            eng.wait_ge(g_mm, n)
                            eng.wait_ge(g_own, eng.snap((c + layer * C) * (T + 1) + t + 1))
                            eng.tensor_scalar(hot_block, iota[:, :], dst_cur[:, 0:1], None,
                                              ALU.is_equal).then_inc(g_hot, 1)
                            eng.wait_ge(g_hot, n)
                            eng.tensor_scalar(dst_cur[:, :], dst_cur[:, :], float(-P), None,
                                              ALU.add).then_inc(g_own, 1)
                            eng.wait_ge(g_mm, eng.snap(n + 1))
                            a = acc[:, bass.ds(t * P, P)]
                            eng.wait_ge(g_add, n)
                            eng.tensor_tensor(a, ps[0][:, 0:P], a, ALU.add).then_inc(g_add, 1)
                        eng.wait_ge(g_own, eng.snap((c + layer * C) * (T + 1) + (T + 1)))
                    eng.wait_ge(g_add, (layer + 1) * C * T + 1)
                    if layer == 0:
                        with eng.Fori(0, G) as g:
                            count_group(g)

                if layer == 0:
                    eng.wait_ge(s_ri, 1)
                else:
                    eng.wait_ge(s_ab, layer * T)
                eng.memset(acc[:, :], 0.0).then_inc(s_zero, 1)
                eng.wait_ge(s_zero, layer + 1)
                with eng.If(is_far == 0):
                    fast()
                with eng.Else():
                    general()
                if layer == 0:
                    eng.wait_ge(s_cnt, 1)
                    eng.tensor_scalar(rcount[:, :], ps[CNT][:, 0:T], 1.0, None, ALU.max).then_inc(s_v, 1)
                    eng.wait_ge(s_v, 8)
                    eng.reciprocal(rcount[:, :], rcount[:, :]).then_inc(s_v, 1)
                    eng.wait_ge(s_v, 9)
                eng.sem_inc(s_agg[layer], 1)

            eng.wait_ge(s_const, 6)
            for k in range(1 + bool(REST)):
                eng.wait_ge(s_x, 16 * (k + 1))
            moments(0)
            eng.wait_ge(s_ri_out, 16)
            with eng.Fori(0, T // 2) as i:
                for u in range(2):
                    keep_self(0, i, u)
            eng.wait_ge(s_yd, T + 2)
            aggregate(0)
            with eng.Fori(0, T // 2) as i:
                for u in range(2):
                    t = i * 2 + u
                    eng.wait_ge(s_pp, eng.snap(i * 2 + (2 + u + 1)))
                    eng.wait_ge(s_h, eng.snap(i * 2 + (T - 2 + u + 1)))
                    eng.scalar_tensor_tensor(out=pre[u][:, :], in0=ps[4 + u][:, 0:P], scalar=rcount[:, bass.ds(t, 1)],
                                             in1=self_term[:, bass.ds(t * P, P)],
                                             op0=ALU.mult, op1=ALU.add).then_inc(s_pre, 1)
                for u in range(2):
                    keep_self(1, i, u)
            eng.wait_ge(s_yd, 2 * T + 2)
            aggregate(1)
            with eng.Fori(0, T // 2) as i:
                for u in range(2):
                    t = i * 2 + u
                    eng.wait_ge(s_pp, eng.snap(i * 2 + (T + 2 + u + 1)))
                    xt = xs[:, bass.ds(t * P, P)]
                    eng.scalar_tensor_tensor(out=xt, in0=ps[4 + u][:, 0:P], scalar=rcount[:, bass.ds(t, 1)],
                                             in1=xt, op0=ALU.mult, op1=ALU.add).then_inc(s_pre, 1)
            eng.wait_ge(s_pre, 2 * T + 2)
            moments(1)
            with eng.Fori(0, T // 2) as i:
                for u in range(2):
                    keep_self(2, i, u)
            eng.wait_ge(s_yd, 3 * T + 2)
            aggregate(2)
            with eng.Fori(0, T // 2) as i:
                for u in range(2):
                    t = i * 2 + u
                    eng.wait_ge(s_pp, eng.snap(i * 2 + (2 * T + 2 + u + 1)))
                    eng.wait_ge(s_h, eng.snap(i * 2 + (3 * T - 2 + u + 1)))
                    eng.tensor_tensor(pre[u][:, :], ps[4 + u][:, 0:P], self_term[:, bass.ds(t * P, P)],
                                      ALU.add).then_inc(s_pre, 1)
                for u in range(2):
                    t = i * 2 + u
                    eng.wait_ge(s_pre, eng.snap(i * 2 + (2 * T + 2 + u + 1)))
                    eng.wait_ge(s_out[u], eng.snap(i * 16 + 16))
                    eng.scalar_tensor_tensor(out=h[u][:, :], in0=pre[u][:, :], scalar=0.0,
                                             in1=xs[:, bass.ds(t * P, P)],
                                             op0=ALU.max, op1=ALU.add).then_inc(s_h, 1)


def kernel(x, src, dst, edge_type_16, L0_gnn_W1_l, L0_gnn_W1_r, L0_gnn_b1, L0_gnn_W2_l, L0_gnn_W2_r, L0_gnn_b2,
           L1_gnn_relation_weights, L1_gnn_self_weight, L1_gnn_bias):
    import numpy as np
    import concourse.bacc as bacc
    from concourse.bass_utils import run_bass_kernel_spmd

    by_chunk = lambda a: np.ascontiguousarray(np.asarray(a).reshape(-1, P).T)
    turned = lambda a: np.ascontiguousarray(np.asarray(a).T)
    arrays = {
        "in_x": np.ascontiguousarray(x),
        "in_src": by_chunk(src), "in_dst": by_chunk(dst), "in_type": by_chunk(edge_type_16),
        "in_w1l": turned(L0_gnn_W1_l), "in_w1r": turned(L0_gnn_W1_r), "in_b1": np.asarray(L0_gnn_b1).reshape(1, P),
        "in_w2l": turned(L0_gnn_W2_l), "in_w2r": turned(L0_gnn_W2_r), "in_b2": np.asarray(L0_gnn_b2).reshape(1, P),
        "in_wrel": np.ascontiguousarray(np.asarray(L1_gnn_relation_weights).reshape(-1, P)),
        "in_wself": np.ascontiguousarray(L1_gnn_self_weight), "in_bias": np.asarray(L1_gnn_bias).reshape(1, P),
    }
    nc = bacc.Bacc("TRN2", target_bir_lowering=False, num_devices=1)
    args = [nc.dram_tensor(n, a.shape, mybir.dt.from_np(a.dtype), kind="ExternalInput").ap() for n, a in arrays.items()]
    args.append(nc.dram_tensor("out_x", arrays["in_x"].shape, F32, kind="ExternalOutput").ap())
    gnn_kernel(nc, *args)
    return run_bass_kernel_spmd(nc, [arrays], core_ids=[0]).results[0]["out_x"]
```

```python
from contextlib import ExitStack

import concourse.bass as bass
from concourse import mybir

ALU = mybir.AluOpType
ACT = mybir.ActivationFunctionType
AX = mybir.AxisListType
DVE = mybir.EngineType.DVE
F32 = mybir.dt.float32
BF16 = mybir.dt.bfloat16
I32 = mybir.dt.int32

P = 128
WIN = 32
BANK = 512
EPS = 1e-5


def chunks_per_group(n_chunks):
    return max(k for k in (25, 20, 15, 10, 5) if n_chunks % k == 0)


def gnn_kernel(nc, x, src, dst, edge_type, w1l, w1r, b1, w2l, w2r, b2, w_rel, w_self, bias, out):
    N = x.shape[0]
    C = src.shape[1]
    K = chunks_per_group(C)
    G = C // K
    HALF = [(0, K // 2), (K // 2, K)]
    NR = w_rel.shape[0] // P
    RB = NR * P // BANK
    T = 2 * -(-N // (2 * P))
    FULL = N // P
    REST = N - FULL * P
    PAIRS = T // 2
    EARLY = min(5, G - PAIRS - 1)
    ROUND = max(k for k in range(1, 8) if PAIRS % k == 0 and (k == 1 or 2 * k * P <= 2 * C))
    PASSES = PAIRS // ROUND
    PASS_HALVES = max(0, 2 * EARLY - 4)
    PASS_STEP = PASSES // (PASS_HALVES + 1)
    PASSES_FIRST = PASSES - PASS_HALVES * PASS_STEP
    X_LOADS = 4

    table = nc.dram_tensor("table", (T * P, P), F32, kind="Internal").ap()
    table2 = nc.dram_tensor("table2", (T * P, P), F32, kind="Internal").ap()
    table_rel = nc.dram_tensor("table_rel", (T * P * NR, P), F32, kind="Internal").ap()
    rel_index = nc.dram_tensor("rel_index", (P, C), I32, kind="Internal").ap()
    table_rel_blocks = table_rel.rearrange("(t p r) f -> t p (r f)", p=P, r=NR)

    ctx = ExitStack()
    with ctx:
        def sb(name, shape, dt):
            return ctx.enter_context(nc.sbuf_tensor(name, shape, dt))

        def sem(name):
            return ctx.enter_context(nc.semaphore(name))

        xs = sb("xs", [P, T * P], F32)
        self_term = sb("self_term", [P, T * P], F32)
        acc = sb("acc", [P, T * P + WIN], F32)
        rows = sb("rows", [P, K * P], F32)
        onehot = sb("onehot", [P, K, WIN], F32)
        dst_i = sb("dst_i", [P, C], I32)
        dst_rel = sb("dst_rel", [P, C], BF16)
        index = sb("index", [P, K], I32)
        iota = sb("iota", [P, P], BF16)
        ident = sb("ident", [P, P], F32)
        W1l, W1r, W2l, W2r, Wself = (sb(n, [P, P], F32) for n in ("W1l", "W1r", "W2l", "W2r", "Wself"))
        Wrel = sb("Wrel", [P, NR * P], F32)
        bias_rows = sb("bias_rows", [1, 3 * P], F32)
        ones_row = sb("ones_row", [1, P], F32)
        zero = sb("zero", [P, 1], F32)
        stats = sb("stats", [P, 2, 6], F32)
        moments_pair = sb("moments_pair", [P, 2, 2], F32)
        rstd_pair = sb("rstd_pair", [P, 2], F32)
        shift_pair = sb("shift_pair", [P, 2], F32)
        eps = sb("eps", [P, 1], F32)
        rcount = sb("rcount", [P, T], F32)
        rel_out = sb("rel_out", [P, NR * P], F32)
        acc_block = [sb(f"acc_block{u}", [P, P], F32) for u in range(2)]
        pre = acc_block
        h = [sb(f"h{u}", [P, P], F32) for u in range(2)]
        hT = [sb(f"hT{u}", [P, P], F32) for u in range(2)]
        dst_hi_i = sb("dst_hi_i", [P, K], I32)
        dst_lo_i = sb("dst_lo_i", [P, K], I32)
        CC = 5
        dst_hi = sb("dst_hi", [P, K], F32)
        dst_lo = sb("dst_lo", [P, K], F32)
        early_rstd = sb("early_rstd", [P, K], F32)
        dst_cur = sb("dst_cur", [P, 1], F32)
        reach = sb("reach", [P, 5], F32)
        far_row = sb("far_row", [1, 1], F32)
        far = sb("far", [1, 1], I32)
        pair_now = sb("pair_now", [1, G + 1], I32)
        pair_on = sb("pair_on", [1, G + 1], I32)

        hot_block = onehot[:, :, :].rearrange("p k w -> p (k w)")[:, 0:P]
        hA = [rel_out[:, u * P:(u + 1) * P] for u in range(2)]
        hTA = [rel_out[:, (2 + u) * P:(3 + u) * P] for u in range(2)]
        at = 4 * P
        half_hots = CC * (T + P)
        hots = rel_out[:, at:at + half_hots].bitcast(BF16)
        hot_hi, hot_lo = (
            [hots[:, k * half_hots + a:k * half_hots + b].rearrange("p (c t) -> p c t", c=CC) for k in range(2)]
            for a, b in ((0, CC * T), (CC * T, half_hots)))
        at += half_hots
        rstd = rel_out[:, at:at + T]
        shift = rel_out[:, at + T:at + 2 * T]
        zero_b = rel_out[:, at + 2 * T:at + 2 * T + P // 2].bitcast(BF16)
        spare = rel_out[:, at + 2 * T + P // 2:at + 2 * T + P // 2 + 16]
        ZERO_CUT = T * P // 2
        cut = [0]

        def scratch(width, parts=slice(0, P)):
            cut.append(cut[-1] + width)
            return self_term[parts, cut[-2]:cut[-1]]

        base_all, type_all, src_all = (scratch(C).bitcast(I32) for _ in range(3))
        h_round = [self_term[:, k * ROUND * P:(k + 1) * ROUND * P] for k in range(2)]
        fall = scratch(-(-C // 2)).bitcast(BF16)[:, 0:C - 1]
        stats_x = scratch(6 * T).rearrange("p (t k) -> p t k", k=6)
        spread = scratch(T)
        var_x = scratch(T)
        early_stats = scratch(6 * K).rearrange("p (t k) -> p t k", k=6)
        early_spread, early_var, early_shift = (scratch(K) for _ in range(3))
        plan = scratch(4 * (G + 1), slice(0, 1)).rearrange("p (k g) -> p k g", k=4)

        ps = [ctx.enter_context(nc.psum_tensor(f"ps{i}", [P, BANK], F32)) for i in range(8)]
        WINDOW_BANKS = [(0, 4, 5, 6, 7), (0, 2, 3), (0, 2, 3, 4, 5)]
        pair_bank = ps[1]
        first_bank = ps[2]
        count_ps = ps[3][:, 0:T]
        rel_ps = ps[4:4 + RB]
        n_ps, t_ps, first_y_ps, first_t_ps = (
            [bank[:, at + u * P:at + (u + 1) * P] for u in range(2)]
            for bank, at in ((pair_bank, 0), (pair_bank, 2 * P), (first_bank, 0), (first_bank, 2 * P)))
        y_ps = n_ps

        s_x = sem("s_x")
        s_dst = sem("s_dst")
        s_setup_in = sem("s_setup_in")
        s_w = sem("s_w")
        s_const = sem("s_const")
        s_ident = sem("s_ident")
        s_v = sem("s_v")
        s_zero = sem("s_zero")
        s_reach = sem("s_reach")
        s_reach_t = sem("s_reach_t")
        s_plan = sem("s_plan")
        s_ri = sem("s_ri")
        s_ri_out = sem("s_ri_out")
        e_stat = sem("e_stat")
        e_v = sem("e_v")
        e_var = sem("e_var")
        e_std = sem("e_std")
        e_norm = sem("e_norm")
        e_h = sem("e_h")
        a_stat = sem("a_stat")
        a_v = sem("a_v")
        a_var = sem("a_var")
        a_std = sem("a_std")
        a_norm = sem("a_norm")
        a_h = sem("a_h")
        a_hst = [sem(f"a_hst{u}") for u in range(2)]
        f_h = sem("f_h")
        f_t = sem("f_t")
        f_hT = sem("f_hT")
        f_y = sem("f_y")
        f_yd = sem("f_yd")
        s_ab = sem("s_ab")
        s_clear = sem("s_clear")
        s_pp = sem("s_pp")
        s_pre = sem("s_pre")
        s_mom = sem("s_mom")
        s_var = sem("s_var")
        s_std = sem("s_std")
        s_norm = sem("s_norm")
        s_h = sem("s_h")
        s_hst = [sem(f"s_hst{u}") for u in range(2)]
        s_tp = sem("s_tp")
        s_hT = sem("s_hT")
        s_y = sem("s_y")
        s_yd = sem("s_yd")
        s_z = sem("s_z")
        s_zc = sem("s_zc")
        s_zst = [sem(f"s_zst{r}") for r in range(RB)]
        s_out = [sem(f"s_out{u}") for u in range(2)]
        s_agg = [sem(f"s_agg{n}") for n in range(3)]
        s_idx = [sem(f"s_idx{i}") for i in range(2)]
        s_row = [sem(f"s_row{j}") for j in range(K)]
        s_mm = [sem(f"s_mm{j}") for j in range(K)]
        s_add = [sem(f"s_add{j}") for j in range(K)]
        s_hot = [sem(f"s_hot{i}") for i in range(2)]
        s_hl = sem("s_hl")
        s_ch = sem("s_ch")
        s_cm = sem("s_cm")
        s_cnt = sem("s_cnt")
        s_deg = sem("s_deg")
        g_idx = sem("g_idx")
        g_row = sem("g_row")
        g_hot = sem("g_hot")
        g_mm = sem("g_mm")
        g_add = sem("g_add")
        g_own = sem("g_own")
        g_clear = sem("g_clear")
        g_free = sem("g_free")
        s_apart = sem("s_apart")

        block = ctx.enter_context(nc.Block())

        def index_source(layer):
            return rel_index if layer == 2 else src

        def gather_table(layer):
            return (table, table2, table_rel)[layer]

        @block.sync
        def _(eng):
            def feed_group(layer, g):
                landed = eng.snap((g + layer * G) * 16)
                for i, (a, b) in enumerate(HALF):
                    eng.wait_ge(s_row[b - 1], landed)
                    eng.sem_inc(s_apart, 1)
                    eng.dma_start(index[:, a:b],
                                  index_source(layer)[:, bass.ds(g * K + a, b - a)]).then_inc(s_idx[i], 16)

            for i, (a, b) in enumerate(HALF):
                eng.dma_start(index[:, a:b], src[:, a:b]).then_inc(s_idx[i], 16)
            for k in range(X_LOADS):
                a, b = FULL * k // X_LOADS, FULL * (k + 1) // X_LOADS
                eng.dma_start(xs[:, a * P:b * P].rearrange("p (t f) -> p t f", f=P),
                              x[a * P:b * P, :].rearrange("(t p) f -> p t f", p=P)).then_inc(s_x, 16)
            if REST:
                eng.wait_ge(s_const, 1)
                eng.dma_start(xs[0:REST, FULL * P:(FULL + 1) * P], x[FULL * P:N, :]).then_inc(s_x, 16)
            for w, a in ((W1l, w1l), (W1r, w1r), (W2l, w2l), (W2r, w2r), (Wself, w_self)):
                eng.dma_start(w[:, :], a).then_inc(s_w, 16)
            eng.dma_start(Wrel[:, :].rearrange("k (r n) -> k r n", n=P),
                          w_rel.rearrange("(r k) n -> k r n", k=P)).then_inc(s_w, 16)
            for n, a in enumerate((b1, b2, bias)):
                eng.dma_start(bias_rows[:, n * P:(n + 1) * P], a).then_inc(s_w, 16)
            for k, s in enumerate([*a_hst, *s_hst, *s_zst, *s_out]):
                eng.dma_start(spare[k:k + 1, :], b1[:, 0:16]).then_inc(s, 16)
            with eng.Fori(1, EARLY) as g:
                feed_group(0, g)
            eng.wait_ge(s_ri, 1)
            eng.dma_start(rel_index, src_all).then_inc(s_ri_out, 16)
            eng.wait_ge(s_plan, 3)
            is_far = eng.value_load(far[0:1, 0:1])
            eng.wait_ge(s_ri_out, 16)

            def feed_indices(layer):
                source = index_source(layer)

                def fast():
                    for i, (a, b) in enumerate(HALF if layer else []):
                        eng.wait_ge(s_row[b - 1], layer * G * 16)
                        eng.dma_start(index[:, a:b], source[:, a:b]).then_inc(s_idx[i], 16)
                    with eng.Fori(1 if layer else EARLY, G) as g:
                        feed_group(layer, g)

                def general():
                    if layer == 0:
                        eng.wait_ge(s_row[0], EARLY * 16)
                    with eng.Fori(0, C) as c:
                        eng.wait_ge(g_free, eng.snap(c + (layer * C + 1)))
                        eng.sem_inc(s_apart, 1)
                        eng.dma_start(index[:, 0:1], source[:, bass.ds(c, 1)],
                                      allow_slow_non_contiguous=True).then_inc(g_idx, 16)

                with eng.If(is_far == 0):
                    fast()
                with eng.Else():
                    general()

            for layer in range(3):
                feed_indices(layer)

        @block.gpsimd
        def _(eng):
            eng.memset(xs[:, FULL * P:T * P], 0.0).then_inc(s_const, 1)
            eng.memset(eps[:, :], EPS).then_inc(s_const, 1)
            eng.iota(iota[:, :], [[1, P]], base=0, channel_multiplier=0,
                     allow_small_or_imprecise_dtypes=True).then_inc(s_const, 1)
            eng.memset(ident[:, :], 1.0).then_inc(s_ident, 1)
            eng.wait_ge(s_ident, 1)
            eng.affine_select(ident[:, :], ident[:, :], [[1, P]], ALU.is_equal, 0.0, base=0,
                              channel_multiplier=-1).then_inc(s_const, 1)
            eng.memset(ones_row[:, :], 1.0).then_inc(s_const, 1)
            eng.memset(zero[:, :], 0.0).then_inc(s_const, 1)
            eng.memset(zero_b[:, :], 0.0).then_inc(s_const, 1)

            def gather_group(tab, layer, g):
                now = eng.snap(g + (layer * G + 1))
                landed = eng.snap((g + (layer * G + 1)) * 16)
                for i, (a, b) in enumerate(HALF):
                    eng.wait_ge(s_idx[i], landed)
                    for j in range(a, b):
                        eng.wait_ge(s_mm[j], now)
                        eng.sem_inc(s_apart, 1)
                        eng.indirect_dma_start(
                            rows[:, j * P:(j + 1) * P], None, tab,
                            bass.IndirectOffsetOnAxis(index[:, j:j + 1], 0)).then_inc(s_row[j], 16)

            with eng.Fori(0, EARLY) as g:
                gather_group(x, 0, g)
            eng.wait_ge(s_plan, 3)
            is_far = eng.value_load(far[0:1, 0:1])

            def gather(layer):
                tab = gather_table(layer)
                stored, filled = [(a_hst, 16 * PASSES + 16), (s_hst, 16 * PAIRS + 16), (s_zst, 16 * T + 16)][layer]
                for s in stored:
                    eng.wait_ge(s, filled)

                def fast():
                    with eng.Fori(0 if layer else EARLY, G) as g:
                        gather_group(tab, layer, g)

                def general():
                    if layer == 0:
                        eng.wait_ge(s_mm[0], EARLY + 1)
                    with eng.Fori(0, C) as c:
                        eng.wait_ge(g_idx, eng.snap((c + (layer * C + 1)) * 16))
                        eng.sem_inc(s_apart, 1)
                        eng.indirect_dma_start(
                            rows[:, 0:P], None, tab,
                            bass.IndirectOffsetOnAxis(index[:, 0:1], 0)).then_inc(g_row, 16)

                with eng.If(is_far == 0):
                    fast()
                with eng.Else():
                    general()

            for layer in range(3):
                gather(layer)

        @block.tensor
        def _(eng):
            for s in [*s_mm, s_cm, g_mm, g_free]:
                eng.sem_inc(s, 1)
            for s in (s_pp, s_tp, s_y, f_t, f_y):
                eng.sem_inc(s, 2)
            eng.sem_inc(s_z, 2 * RB)
            eng.wait_ge(s_const, 7)
            eng.wait_ge(s_reach, 1)
            eng.matmul(pair_bank[0:1, 0:P], reach[:, 2:3], ident[:, :], start=True, stop=True).then_inc(s_reach_t, 1)
            eng.matmul(count_ps, zero_b[:, :], zero_b[:, 0:T], start=True, stop=False, skip_group_check=True)

            def first_self(i):
                m = i * 2
                eng.wait_ge(f_h, eng.snap(m + 2))
                eng.wait_ge(f_yd, eng.snap(m + 2))
                for u in range(2):
                    eng.transpose(first_t_ps[u], hA[u], ident[:, :]).then_inc(f_t, 1)
                eng.wait_ge(f_hT, eng.snap(m + 4))
                for u in range(2):
                    eng.matmul(first_y_ps[u], ones_row[:, :], bias_rows[:, 0:P], start=True, stop=False)
                    eng.matmul(first_y_ps[u], hTA[u], W1r[:, :], start=False, stop=True).then_inc(f_y, 1)

            def pair_products(n, i):
                m = i * 2 + n * T
                eng.wait_ge(s_pre, eng.snap(m + 2))
                eng.wait_ge(s_yd, eng.snap(m + 2) if n < 2 else 2 * T + 2)
                for u in range(2):
                    eng.wait_ge(s_ab, eng.snap(m + (u + 1)))
                    eng.matmul(n_ps[u], acc_block[u][:, :], (W1l, W2l, ident)[n][:, :],
                               start=True, stop=True).then_inc(s_pp, 1)
                if n == 2:
                    return
                eng.wait_ge(s_h, eng.snap(m + 4))
                for u in range(2):
                    eng.transpose(t_ps[u], h[u][:, :], ident[:, :]).then_inc(s_tp, 1)
                eng.wait_ge(s_hT, eng.snap(m + 2))
                for u in range(2):
                    eng.matmul(y_ps[u], ones_row[:, :], bias_rows[:, (n + 1) * P:(n + 2) * P], start=True, stop=False)
                    eng.matmul(y_ps[u], hT[u][:, :], (W2r, Wself)[n][:, :], start=False, stop=True).then_inc(s_y, 1)
                for u in range(2 if n == 1 else 0):
                    for r in range(RB):
                        eng.wait_ge(s_zc, eng.snap(i * (2 * RB) + (u * RB + r + 1)))
                        eng.matmul(rel_ps[r][:, :], hT[u][:, :], Wrel[:, r * BANK:(r + 1) * BANK],
                                   start=True, stop=True).then_inc(s_z, 1)

            def count_products(g, q):
                eng.wait_ge(s_ch, eng.snap(g * (K // CC) + (q + 1)))
                for j in range(CC):
                    mm = eng.matmul(count_ps, hot_lo[q % 2][:, j, :], hot_hi[q % 2][:, j, :],
                                    start=False, stop=False, skip_group_check=True)
                mm.then_inc(s_cm, 1)

            def window_products(layer, g, early):
                banks = WINDOW_BANKS[layer]
                NB = len(banks)
                now = eng.snap(g + (layer * G + 1))
                after = eng.snap(g + (layer * G + 2))
                landed = eng.snap((g + (layer * G + 1)) * 16)
                for half, (a, b) in enumerate(HALF):
                    eng.wait_ge(s_hot[half], now)
                    for j in range(a, b):
                        if early:
                            eng.wait_ge(e_h, eng.snap(g * K + (j + 1)))
                        else:
                            eng.wait_ge(s_row[j], landed)
                        if j >= NB:
                            eng.wait_ge(s_add[j - NB], after)
                        else:
                            eng.wait_ge(s_add[max(k for k in range(K) if k % NB == j)], now)
                        eng.matmul(ps[banks[j % NB]][:, 0:WIN], rows[:, j * P:(j + 1) * P], onehot[:, j, :],
                                   start=True, stop=True).then_inc(s_mm[j], 1)
                        if layer == 0 and j >= CC and j % CC == CC // 2:
                            count_products(g, j // CC - 1)
                if layer == 0:
                    count_products(g, K // CC - 1)

            def aggregate(layer):
                def group(g):
                    window_products(layer, g, False)
                    on = eng.value_load(pair_on[0:1, bass.ds(g, 1)], min_val=0, max_val=1)
                    i = eng.value_load(pair_now[0:1, bass.ds(g, 1)], min_val=0, max_val=PAIRS - 2)
                    with eng.If(on > 0):
                        pair_products(layer, i)

                def fast():
                    if layer == 0:
                        with eng.Fori(0, PAIRS) as i:
                            first_self(i)
                            group(eng.snap(i + EARLY))
                    with eng.Fori(0 if layer else EARLY + PAIRS, G) as g:
                        group(g)

                def general():
                    if layer == 0:
                        with eng.Fori(0, PAIRS) as i:
                            first_self(i)
                        eng.wait_ge(s_add[K - 1], EARLY + 1)
                    with eng.Fori(0, C) as c:
                        landed = eng.snap((c + (layer * C + 1)) * 16)
                        with eng.Fori(0, T) as t:
                            n = eng.snap((c + layer * C) * T + t + 1)
                            eng.wait_ge(g_row, landed)
                            eng.wait_ge(g_hot, n)
                            eng.wait_ge(g_add, n)
                            eng.matmul(ps[0][:, 0:P], rows[:, 0:P], hot_block, start=True, stop=True).then_inc(g_mm, 1)
                        eng.wait_ge(g_mm, eng.snap((c + (layer * C + 1)) * T + 1))
                        eng.sem_inc(g_free, 1)
                    if layer == 0:
                        with eng.Fori(EARLY, G) as g:
                            for q in range(K // CC):
                                count_products(g, q)

                if layer:
                    eng.wait_ge(s_agg[layer - 1], 1)
                    eng.wait_ge(s_deg, T)
                    eng.wait_ge(f_yd, T + 2)
                    if layer == 2:
                        eng.wait_ge(s_zc, RB * T + RB)
                with eng.If(is_far == 0):
                    fast()
                with eng.Else():
                    general()
                if layer == 0:
                    eng.matmul(count_ps, zero_b[:, :], zero_b[:, 0:T], start=False, stop=True,
                               skip_group_check=True).then_inc(s_cnt, 1)
                with eng.Fori(rest_from, PAIRS) as i:
                    pair_products(layer, i)

            with eng.Fori(0, EARLY) as g:
                window_products(0, g, True)
            eng.wait_ge(s_w, 16 * 9)
            eng.wait_ge(s_plan, 3)
            is_far = eng.value_load(far[0:1, 0:1])
            rest_from = eng.value_load(pair_now[0:1, G:G + 1], min_val=0, max_val=PAIRS - 1)
            for layer in range(3):
                aggregate(layer)

        @block.scalar
        def _(eng):
            eng.dma_start(dst_i[:, :], dst).then_inc(s_dst, 16)
            eng.dma_start(base_all, dst[0:1, :].broadcast_to([P, C])).then_inc(s_dst, 16)
            eng.dma_start(src_all, src).then_inc(s_setup_in, 16)
            eng.dma_start(type_all, edge_type).then_inc(s_setup_in, 16)
            for s in (s_h, f_hT):
                eng.sem_inc(s, 2)
            eng.sem_inc(s_zc, RB)
            eng.wait_ge(s_const, 7)
            eng.activation(acc[:, 0:ZERO_CUT], zero[:, 0:1].broadcast_to([P, ZERO_CUT]), ACT.Copy).then_inc(s_zero, 1)

            def norm_first(out_tile, t):
                return eng.activation(out_tile, xs[:, bass.ds(t * P, P)], ACT.Relu, bias=shift[:, bass.ds(t, 1)],
                                      scale=rstd[:, bass.ds(t, 1)])

            def table_rows(r):
                for k in range(2):
                    eng.wait_ge(a_hst[k], eng.snap(r * 16 + 16))
                    eng.sem_inc(s_apart, 1)
                    for u in range(ROUND):
                        norm_first(h_round[k][:, u * P:(u + 1) * P],
                                   r * (2 * ROUND) + (k * ROUND + u)).then_inc(a_h, 1)
                    row = eng.snap((r * (2 * ROUND) + k * ROUND) * P)
                    eng.wait_ge(a_h, eng.snap(r * (2 * ROUND) + (k + 1) * ROUND))
                    eng.dma_start(table[bass.ds(row, ROUND * P), :].rearrange("(t p) f -> p t f", p=P),
                                  h_round[k].rearrange("p (t f) -> p t f", f=P)).then_inc(a_hst[k], 16)

            def normalise_rows(g, with_table):
                for half, (a, b) in enumerate(HALF):
                    n = eng.snap(g * 2 + (half + 1))
                    eng.wait_ge(e_var, n)
                    eng.activation(early_rstd[:, a:b], early_var[:, a:b], ACT.Sqrt, bias=eps[:, 0:1],
                                   scale=1.0 / P).then_inc(e_std, 1)
                    eng.wait_ge(e_norm, n)
                    eng.sem_inc(s_apart, 1)
                    for j in range(a, b):
                        slot = rows[:, j * P:(j + 1) * P]
                        eng.activation(slot, slot, ACT.Relu, bias=early_shift[:, j:j + 1],
                                       scale=early_rstd[:, j:j + 1]).then_inc(e_h, 1)
                    if with_table and PASS_STEP:
                        with eng.Fori(0, PASS_STEP) as i:
                            table_rows(eng.snap((g - 1) * (2 * PASS_STEP) + (half * PASS_STEP + PASSES_FIRST) + i))

            normalise_rows(0, False)
            eng.wait_ge(a_var, 1)
            eng.activation(rstd, var_x, ACT.Sqrt, bias=eps[:, 0:1], scale=1.0 / P).then_inc(a_std, 1)
            eng.wait_ge(a_norm, 1)
            if 2 * ROUND * P > C:
                eng.wait_ge(s_ri, 1)
            with eng.Fori(0, PASSES_FIRST) as r:
                table_rows(r)
            if EARLY > 2:
                with eng.Fori(1, EARLY - 1) as g:
                    normalise_rows(g, True)
            if EARLY > 1:
                normalise_rows(EARLY - 1, False)
            eng.wait_ge(s_plan, 3)
            is_far = eng.value_load(far[0:1, 0:1])
            rest_from = eng.value_load(pair_now[0:1, G:G + 1], min_val=0, max_val=PAIRS - 1)
            for s in a_hst:
                eng.wait_ge(s, 16 * PASSES + 16)

            def first_self(i):
                eng.wait_ge(f_t, eng.snap(i * 2 + 2))
                eng.sem_inc(s_apart, 1)
                for u in range(2):
                    norm_first(hA[u], i * 2 + u).then_inc(f_h, 1)
                eng.wait_ge(f_t, eng.snap(i * 2 + 4))
                eng.wait_ge(f_y, eng.snap(i * 2 + 2))
                for u in range(2):
                    eng.activation(hTA[u], first_t_ps[u], ACT.Copy).then_inc(f_hT, 1)

            def copy_acc(n, i):
                for u in range(2):
                    m = i * 2 + (n * T + u)
                    block_acc = acc[:, bass.ds((i * 2 + u) * P, P)]
                    eng.wait_ge(s_pp, eng.snap(m + 1))
                    if n == 2:
                        eng.wait_ge(s_h, eng.snap(m + 1))
                    eng.sem_inc(s_apart, 1)
                    eng.activation(acc_block[u][:, :], block_acc, ACT.Copy).then_inc(s_ab, 1)
                if n < 2:
                    for u in range(2):
                        m = i * 2 + (n * T + u)
                        eng.wait_ge(s_ab, eng.snap(m + 1))
                        eng.sem_inc(s_apart, 1)
                        eng.activation(acc[:, bass.ds((i * 2 + u) * P, P)], zero[:, 0:1].broadcast_to([P, P]),
                                       ACT.Copy).then_inc(s_clear, 1)

            def pair_steps(n, i):
                copy_acc(n, i)
                if n == 2:
                    for u in range(2):
                        row = eng.snap((i * 2 + u) * P)
                        eng.wait_ge(s_h, eng.snap(i * 2 + (n * T + u + 3)))
                        eng.dma_start(out[bass.ds(row, P), :], h[u][:, :]).then_inc(s_out[u], 16)
                    return
                if n == 1:
                    eng.wait_ge(s_var, eng.snap(i + 1))
                    eng.activation(rstd_pair[:, :], moments_pair[:, :, 1], ACT.Sqrt, bias=eps[:, 0:1],
                                   scale=1.0).then_inc(s_std, 1)
                    eng.wait_ge(s_norm, eng.snap(i + 1))
                for u in range(2):
                    m = i * 2 + (n * T + u)
                    eng.wait_ge(s_tp, eng.snap(m + 1))
                    if n == 0:
                        eng.wait_ge(s_hst[u], eng.snap(i * 16 + 16))
                        eng.wait_ge(s_pre, eng.snap(m + 3))
                        eng.activation(h[u][:, :], pre[u][:, :], ACT.Relu).then_inc(s_h, 1)
                    else:
                        eng.sem_inc(s_apart, 1)
                        eng.activation(h[u][:, :], xs[:, bass.ds((i * 2 + u) * P, P)], ACT.Relu,
                                       bias=shift_pair[:, u:u + 1], scale=rstd_pair[:, u:u + 1]).then_inc(s_h, 1)
                if n == 0:
                    for u in range(2):
                        row = eng.snap((i * 2 + u) * P)
                        eng.wait_ge(s_h, eng.snap(i * 2 + (u + 3)))
                        eng.dma_start(table2[bass.ds(row, P), :], h[u][:, :]).then_inc(s_hst[u], 16)
                m = i * 2 + n * T
                eng.wait_ge(s_tp, eng.snap(m + 4))
                eng.wait_ge(s_y, eng.snap(m + 2))
                if n == 1:
                    eng.wait_ge(s_z, eng.snap((i + 1) * (2 * RB)))
                for u in range(2):
                    eng.activation(hT[u][:, :], t_ps[u], ACT.Copy).then_inc(s_hT, 1)
                if n == 1:
                    banks = [(u, r) for u in range(2) for r in range(RB)]

                    def copy_bank(u, r):
                        eng.wait_ge(s_z, eng.snap(i * (2 * RB) + (2 * RB + u * RB + r + 1)))
                        eng.wait_ge(s_zst[r], eng.snap(i * 32 + (u + 1) * 16))
                        eng.activation(rel_out[:, r * BANK:(r + 1) * BANK], rel_ps[r][:, :], ACT.Copy).then_inc(s_zc, 1)

                    def store_bank(u, r):
                        part = slice(r * BANK, (r + 1) * BANK)
                        eng.wait_ge(s_zc, eng.snap(i * (2 * RB) + (RB + u * RB + r + 1)))
                        t = eng.snap(i * 2 + u)
                        eng.dma_start(table_rel_blocks[bass.ds(t, 1), :, part].rearrange("t p f -> (t p) f"),
                                      rel_out[:, part]).then_inc(s_zst[r], 16)

                    copy_bank(*banks[0])
                    for last, bank in zip(banks, banks[1:]):
                        copy_bank(*bank)
                        store_bank(*last)
                    store_bank(*banks[-1])

            def aggregate(layer):
                def group(g):
                    on = eng.value_load(pair_on[0:1, bass.ds(g, 1)], min_val=0, max_val=1)
                    i = eng.value_load(pair_now[0:1, bass.ds(g, 1)], min_val=0, max_val=PAIRS - 2)
                    with eng.If(on > 0):
                        eng.wait_ge(s_add[K - 1], eng.snap(g + (layer * G + 2)))
                        pair_steps(layer, i)

                def fast():
                    if layer == 0:
                        with eng.Fori(0, PAIRS) as i:
                            first_self(i)
                            group(eng.snap(i + EARLY))
                    with eng.Fori(0 if layer else EARLY + PAIRS, G) as g:
                        group(g)

                def general():
                    if layer == 0:
                        with eng.Fori(0, PAIRS) as i:
                            first_self(i)
                    eng.wait_ge(s_agg[layer], 1)

                with eng.If(is_far == 0):
                    fast()
                with eng.Else():
                    general()
                eng.wait_ge(s_agg[layer], 1)
                if layer < 2:
                    with eng.Fori(rest_from, PAIRS) as i:
                        pair_steps(layer, i)
                    return
                with eng.If(rest_from < PAIRS - 1):
                    with eng.Fori(rest_from, PAIRS - 1) as i:
                        pair_steps(layer, i)
                copy_acc(2, PAIRS - 1)
                for t in range(T - 2, T):
                    n = min(max(N - t * P, 0), P)
                    if n:
                        eng.wait_ge(s_h, 2 * T + t + 3)
                        eng.dma_start(out[t * P:t * P + n, :], h[t % 2][0:n, :]).then_inc(s_out[t % 2], 16)
                for u in range(2):
                    eng.wait_ge(s_out[u], 16 * len([t for t in range(u, T, 2) if t * P < N]) + 16)

            for layer in range(3):
                aggregate(layer)

        @block.vector
        def _(eng):
            for s in [*s_add, g_add]:
                eng.sem_inc(s, 1)
            for s in (s_yd, s_pre, f_yd):
                eng.sem_inc(s, 2)

            def norms(moments, d, v, r, sh, own, before, var, std, turn, norm):
                even_mean, even_m2 = moments[:, :, 1], moments[:, :, 2]
                odd_mean, odd_m2 = moments[:, :, 4], moments[:, :, 5]
                eng.tensor_tensor(d, even_mean, odd_mean, ALU.subtract).then_inc(own, 1)
                eng.tensor_tensor(v, even_m2, odd_m2, ALU.add).then_inc(own, 1)
                eng.tensor_tensor(sh, even_mean, odd_mean, ALU.add).then_inc(own, 1)
                eng.wait_ge(own, eng.snap(before + 3))
                eng.tensor_tensor(d, d, d, ALU.mult).then_inc(own, 1)
                eng.wait_ge(own, eng.snap(before + 4))
                eng.scalar_tensor_tensor(out=v, in0=d, scalar=P / 4.0, in1=v,
                                         op0=ALU.mult, op1=ALU.add).then_inc(var, 1)
                eng.wait_ge(std, turn)
                eng.reciprocal(r, r).then_inc(own, 1)
                eng.wait_ge(own, eng.snap(before + 5))
                eng.scalar_tensor_tensor(out=sh, in0=sh, scalar=-0.5, in1=r,
                                         op0=ALU.mult, op1=ALU.mult).then_inc(own, 1)
                eng.wait_ge(own, eng.snap(before + 6))
                eng.sem_inc(norm, 1)

            eng.memset(acc[:, ZERO_CUT:], 0.0).then_inc(s_zero, 1)
            eng.wait_ge(s_dst, 32)
            eng.tensor_tensor(dst_rel[:, :], dst_i[:, :], base_all, ALU.subtract).then_inc(s_v, 1)
            eng.tensor_tensor(fall, base_all[:, 0:C - 1], base_all[:, 1:C], ALU.subtract).then_inc(s_v, 1)
            eng.wait_ge(s_v, 2)
            eng.tensor_reduce(reach[:, 0:1], dst_rel[:, :], AX.X, ALU.max).then_inc(s_v, 1)
            eng.tensor_reduce(reach[:, 1:2], dst_rel[:, :], AX.X, ALU.min).then_inc(s_v, 1)
            eng.tensor_reduce(reach[:, 4:5], fall, AX.X, ALU.max).then_inc(s_v, 1)
            eng.wait_ge(s_v, 5)
            eng.tensor_scalar(reach[:, 3:4], reach[:, 0:1], float(WIN - 1), None, ALU.subtract).then_inc(s_v, 1)
            eng.wait_ge(s_v, 6)
            eng.scalar_tensor_tensor(out=reach[:, 3:4], in0=reach[:, 1:2], scalar=-1.0, in1=reach[:, 3:4],
                                     op0=ALU.mult, op1=ALU.max).then_inc(s_v, 1)
            eng.wait_ge(s_v, 7)
            eng.tensor_tensor(reach[:, 2:3], reach[:, 3:4], reach[:, 4:5], ALU.max).then_inc(s_reach, 1)
            eng.memset(pair_on[:, :], 0).then_inc(s_v, 1)
            eng.wait_ge(s_reach_t, 1)
            eng.tensor_reduce(far_row[:, :], pair_bank[0:1, 0:P], AX.X, ALU.max).then_inc(s_v, 1)
            allow, final, done, pick = (plan[:, k, 0:G - 1] for k in range(4))
            eng.tensor_scalar(pair_now[:, 0:G - 1], dst_i[0:1, K:C:K], 8, None,
                              ALU.logical_shift_right).then_inc(s_v, 1)
            eng.memset(allow[:, 0:EARLY], 0.0).then_inc(s_v, 1)
            eng.memset(allow[:, EARLY:G - 1], 1.0).then_inc(s_v, 1)
            eng.wait_ge(s_v, 12)
            eng.tensor_scalar(final, pair_now[:, 0:G - 1], float(PAIRS - 1), None, ALU.min).then_inc(s_v, 1)
            eng.wait_ge(s_v, 13)
            eng.tensor_tensor_scan(done, allow, final, 0.0, ALU.add, ALU.min).then_inc(s_v, 1)
            eng.memset(pick, 0.0).then_inc(s_v, 1)
            eng.wait_ge(s_v, 15)
            eng.tensor_copy(pick[:, 1:G - 1], done[:, 0:G - 2]).then_inc(s_v, 1)
            eng.memset(pair_now[:, :], 0).then_inc(s_v, 1)
            eng.wait_ge(s_v, 17)
            eng.tensor_tensor(pair_on[:, 0:G - 1], done, pick, ALU.subtract).then_inc(s_plan, 1)
            eng.tensor_scalar(pair_now[:, 0:G - 1], pick, float(PAIRS - 2), None, ALU.min).then_inc(s_v, 1)
            eng.tensor_scalar(far[:, :], far_row[:, :], 0.0, None, ALU.max).then_inc(s_plan, 1)
            eng.tensor_scalar(far_row[:, :], far_row[:, :], 0.0, None, ALU.is_le).then_inc(s_v, 1)
            eng.wait_ge(s_v, 19)
            eng.tensor_tensor(pair_now[:, G:G + 1], done[:, G - 2:G - 1], far_row[:, :], ALU.mult).then_inc(s_plan, 1)
            eng.wait_ge(s_const, 7)

            def first_self(i):
                eng.wait_ge(f_y, eng.snap(i * 2 + 4))
                for u in range(2):
                    eng.tensor_copy(self_term[:, bass.ds((i * 2 + u) * P, P)], first_y_ps[u]).then_inc(f_yd, 1)

            def in_degrees(i):
                r = rcount[:, bass.ds(i * 2, 2)]
                eng.tensor_scalar(r, count_ps[:, bass.ds(i * 2, 2)], 1.0, None, ALU.max).then_inc(s_deg, 1)
                eng.wait_ge(s_deg, eng.snap(i * 2 + 1))
                eng.sem_inc(s_apart, 1)
                eng.reciprocal(r, r).then_inc(s_deg, 1)
                eng.wait_ge(s_deg, eng.snap(i * 2 + 2))

            def pair_moments(i):
                for u in range(2):
                    eng.wait_ge(s_pre, eng.snap(i * 2 + (T + u + 3)))
                    eng.sem_inc(s_apart, 1)
                    eng.bn_stats(stats[:, u, :], xs[:, bass.ds((i * 2 + u) * P, P)]).then_inc(s_mom, 1)
                eng.wait_ge(s_mom, eng.snap(i * 6 + 2))
                eng.sem_inc(s_apart, 1)
                eng.bn_aggr(moments_pair[:, 0, :], stats[:, 0, :]).then_inc(s_mom, 1)
                eng.bn_aggr(moments_pair[:, 1, :], stats[:, 1, :]).then_inc(s_mom, 1)
                eng.wait_ge(s_mom, eng.snap(i * 6 + 4))
                eng.sem_inc(s_var, 1)
                eng.wait_ge(s_std, eng.snap(i + 1))
                eng.reciprocal(rstd_pair[:, :], rstd_pair[:, :]).then_inc(s_mom, 1)
                eng.wait_ge(s_mom, eng.snap(i * 6 + 5))
                eng.scalar_tensor_tensor(out=shift_pair[:, :], in0=moments_pair[:, :, 0], scalar=-1.0,
                                         in1=rstd_pair[:, :], op0=ALU.mult, op1=ALU.mult).then_inc(s_mom, 1)
                eng.wait_ge(s_mom, eng.snap(i * 6 + 6))
                eng.sem_inc(s_norm, 1)

            def pair_steps(n, i):
                if n == 0:
                    in_degrees(i)
                eng.wait_ge(s_pp, eng.snap(i * 2 + (n * T + 4)))
                for u in range(2):
                    m = i * 2 + (n * T + u)
                    block_of = lambda a: a[:, bass.ds((i * 2 + u) * P, P)]
                    if n == 0:
                        eng.wait_ge(s_h, eng.snap(m + 1))
                        eng.scalar_tensor_tensor(out=pre[u][:, :], in0=n_ps[u], scalar=rcount[:, bass.ds(i * 2 + u, 1)],
                                                 in1=block_of(self_term), op0=ALU.mult, op1=ALU.add).then_inc(s_pre, 1)
                    elif n == 1:
                        eng.scalar_tensor_tensor(out=block_of(xs), in0=n_ps[u], scalar=rcount[:, bass.ds(i * 2 + u, 1)],
                                                 in1=block_of(xs), op0=ALU.mult, op1=ALU.add).then_inc(s_pre, 1)
                    else:
                        eng.wait_ge(s_h, eng.snap(m + 1))
                        eng.tensor_tensor(pre[u][:, :], n_ps[u], block_of(self_term), ALU.add).then_inc(s_pre, 1)
                if n == 1:
                    pair_moments(i)
                if n < 2:
                    eng.wait_ge(s_y, eng.snap(i * 2 + (n * T + 4)))
                for u in range(2):
                    m = i * 2 + (n * T + u)
                    block_of = lambda a: a[:, bass.ds((i * 2 + u) * P, P)]
                    if n == 2:
                        eng.wait_ge(s_pre, eng.snap(m + 3))
                        eng.wait_ge(s_out[u], eng.snap(i * 16 + 16))
                        eng.scalar_tensor_tensor(out=h[u][:, :], in0=pre[u][:, :], scalar=0.0, in1=block_of(xs),
                                                 op0=ALU.max, op1=ALU.add).then_inc(s_h, 1)
                        continue
                    if n == 0:
                        eng.tensor_tensor(block_of(xs), y_ps[u], block_of(xs), ALU.add).then_inc(s_yd, 1)
                    else:
                        eng.tensor_copy(block_of(self_term), y_ps[u]).then_inc(s_yd, 1)

            def split_dst(g):
                d = dst_i[:, bass.ds(g * K, K)]
                eng.wait_ge(s_cm, eng.snap(g * (K // CC) + 1))
                eng.tensor_scalar(dst_hi_i[:, :], d, 7, None, ALU.logical_shift_right).then_inc(s_hl, 1)
                eng.tensor_scalar(dst_lo_i[:, :], d, P - 1, None, ALU.bitwise_and).then_inc(s_hl, 1)
                eng.wait_ge(s_hl, eng.snap(g * 4 + 2))
                eng.tensor_copy(dst_hi[:, :], dst_hi_i[:, :]).then_inc(s_hl, 1)
                eng.tensor_copy(dst_lo[:, :], dst_lo_i[:, :]).then_inc(s_hl, 1)
                eng.wait_ge(s_hl, eng.snap(g * 4 + 4))

            def count_onehot(g, j):
                q = j // CC
                if j % CC == 0:
                    eng.wait_ge(s_cm, eng.snap(g * (K // CC) + max(q, 1)))
                eng.tensor_scalar(hot_hi[q % 2][:, j % CC, :], iota[:, 0:T], dst_hi[:, j:j + 1], None, ALU.is_equal)
                lo = eng.tensor_scalar(hot_lo[q % 2][:, j % CC, :], iota[:, :], dst_lo[:, j:j + 1], None, ALU.is_equal)
                if j % CC == CC - 1:
                    lo.then_inc(s_ch, 1)

            def early_moments(g, a, b):
                landed = eng.snap((g + 1) * 16)
                for j in range(a, b):
                    eng.wait_ge(s_row[j], landed)
                    eng.sem_inc(s_apart, 1)
                    eng.bn_stats(early_stats[:, j, :], rows[:, j * P:(j + 1) * P]).then_inc(e_stat, 1)

            def early_norms(g, half, a, b):
                eng.wait_ge(e_stat, eng.snap(g * K + b))
                norms(early_stats[:, a:b, :], early_spread[:, a:b], early_var[:, a:b], early_rstd[:, a:b],
                      early_shift[:, a:b], e_v, g * 12 + half * 6, e_var, e_std, eng.snap(g * 2 + (half + 1)), e_norm)

            def add_windows(layer, g, early, with_x=False):
                banks = WINDOW_BANKS[layer]
                now = eng.snap(g + (layer * G + 1))
                after = eng.snap(g + (layer * G + 2))
                for k, (a, b) in enumerate(HALF):
                    eng.wait_ge(s_mm[b - 1], now)
                    eng.tensor_tensor(
                        onehot[:, a:b, :], iota[:, 0:WIN].unsqueeze(1).broadcast_to([P, b - a, WIN]),
                        dst_rel[:, bass.ds(g * K + a, b - a)].unsqueeze(2).broadcast_to([P, b - a, WIN]),
                        ALU.is_equal).then_inc(s_hot[k], 1)
                _, base = nc.values_load_multi_w_load_instructions(
                    dst_i[0:1, bass.ds(g * K, K)], engines=(DVE,), min_val=0, max_val=N - 1)
                if layer == 0:
                    split_dst(g)
                for k, (a, b) in enumerate(HALF):
                    if early:
                        if k == 0:
                            early_moments(g, a, b)
                        early_norms(g, k, a, b)
                        if k == 0:
                            early_moments(g, *HALF[1])
                    for j in range(a, b):
                        if early and j == 0:
                            eng.wait_ge(s_zero, 2)
                        eng.wait_ge(s_mm[j], after)
                        eng.wait_ge(s_add[j - 1], after if j else now)
                        window = acc[:, bass.ds(base[j], WIN)]
                        eng.tensor_tensor(window, ps[banks[j % len(banks)]][:, 0:WIN], window,
                                          ALU.add).then_inc(s_add[j], 1)
                        if layer == 0:
                            count_onehot(g, j)
                        if with_x:
                            if j == 0:
                                eng.wait_ge(s_x, 16 * (X_LOADS + (1 if REST else 0)))
                            for t in range(T * j // K, T * (j + 1) // K):
                                x_moments(t)

            def x_moments(t):
                eng.bn_stats(stats_x[:, t, :], xs[:, t * P:(t + 1) * P]).then_inc(a_stat, 1)

            def aggregate(layer):
                def group(g):
                    add_windows(layer, g, False)
                    on = eng.value_load(pair_on[0:1, bass.ds(g, 1)], min_val=0, max_val=1)
                    i = eng.value_load(pair_now[0:1, bass.ds(g, 1)], min_val=0, max_val=PAIRS - 2)
                    with eng.If(on > 0):
                        if layer == 0:
                            eng.wait_ge(s_cm, eng.snap(g * (K // CC) + (K // CC + 1)))
                        pair_steps(layer, i)

                def fast():
                    if layer == 0:
                        with eng.Fori(0, PAIRS) as i:
                            first_self(i)
                            group(eng.snap(i + EARLY))
                    with eng.Fori(0 if layer else EARLY + PAIRS, G) as g:
                        group(g)
                    eng.wait_ge(s_add[K - 1], (layer + 1) * G + 1)

                def general():
                    if layer == 0:
                        with eng.Fori(0, PAIRS) as i:
                            first_self(i)
                        eng.memset(acc[:, :], 0.0).then_inc(g_clear, 1)
                        eng.wait_ge(g_clear, 1)
                    with eng.Fori(0, C) as c:
                        eng.wait_ge(g_mm, eng.snap((c + layer * C) * T + 1))
                        eng.tensor_copy(dst_cur[:, :], dst_i[:, bass.ds(c, 1)]).then_inc(g_own, 1)
                        with eng.Fori(0, T) as t:
                            n = eng.snap((c + layer * C) * T + t + 1)
                            eng.wait_ge(g_mm, n)
                            eng.wait_ge(g_own, eng.snap((c + layer * C) * (T + 1) + t + 1))
                            eng.tensor_scalar(hot_block, iota[:, :], dst_cur[:, 0:1], None,
                                              ALU.is_equal).then_inc(g_hot, 1)
                            eng.wait_ge(g_hot, n)
                            eng.tensor_scalar(dst_cur[:, :], dst_cur[:, :], float(-P), None,
                                              ALU.add).then_inc(g_own, 1)
                            eng.wait_ge(g_mm, eng.snap(n + 1))
                            a = acc[:, bass.ds(t * P, P)]
                            eng.wait_ge(g_add, n)
                            eng.tensor_tensor(a, ps[0][:, 0:P], a, ALU.add).then_inc(g_add, 1)
                        eng.wait_ge(g_own, eng.snap((c + layer * C) * (T + 1) + (T + 1)))
                    eng.wait_ge(g_add, (layer + 1) * C * T + 1)
                    if layer == 0:
                        with eng.Fori(EARLY, G) as g:
                            split_dst(g)
                            for j in range(K):
                                count_onehot(g, j)

                if layer == 0:
                    eng.wait_ge(s_ri_out, 16)
                else:
                    eng.wait_ge(s_clear, layer * T)
                with eng.If(is_far == 0):
                    fast()
                with eng.Else():
                    general()
                if layer == 0:
                    eng.wait_ge(s_cnt, 1)
                eng.sem_inc(s_agg[layer], 1)
                with eng.Fori(rest_from, PAIRS) as i:
                    pair_steps(layer, i)

            add_windows(0, 0, True, True)
            eng.wait_ge(a_stat, T)
            norms(stats_x, spread, var_x, rstd, shift, a_v, 0, a_var, a_std, 1, a_norm)
            eng.wait_ge(s_setup_in, 32)
            eng.scalar_tensor_tensor(out=src_all, in0=src_all, scalar=float(NR), in1=type_all,
                                     op0=ALU.mult, op1=ALU.add).then_inc(s_ri, 1)
            with eng.Fori(1, EARLY) as g:
                add_windows(0, g, True)
            eng.wait_ge(s_add[K - 1], EARLY + 1)
            eng.wait_ge(s_plan, 3)
            is_far = eng.value_load(far[0:1, 0:1])
            rest_from = eng.value_load(pair_now[0:1, G:G + 1], min_val=0, max_val=PAIRS - 1)
            for layer in range(3):
                aggregate(layer)


def kernel(x, src, dst, edge_type_16, L0_gnn_W1_l, L0_gnn_W1_r, L0_gnn_b1, L0_gnn_W2_l, L0_gnn_W2_r, L0_gnn_b2,
           L1_gnn_relation_weights, L1_gnn_self_weight, L1_gnn_bias):
    import numpy as np
    import concourse.bacc as bacc
    from concourse.bass_utils import run_bass_kernel_spmd

    by_chunk = lambda a: np.ascontiguousarray(np.asarray(a).reshape(-1, P).T)
    turned = lambda a: np.ascontiguousarray(np.asarray(a).T)
    arrays = {
        "in_x": np.ascontiguousarray(x),
        "in_src": by_chunk(src), "in_dst": by_chunk(dst), "in_type": by_chunk(edge_type_16),
        "in_w1l": turned(L0_gnn_W1_l), "in_w1r": turned(L0_gnn_W1_r), "in_b1": np.asarray(L0_gnn_b1).reshape(1, P),
        "in_w2l": turned(L0_gnn_W2_l), "in_w2r": turned(L0_gnn_W2_r), "in_b2": np.asarray(L0_gnn_b2).reshape(1, P),
        "in_wrel": np.ascontiguousarray(np.asarray(L1_gnn_relation_weights).reshape(-1, P)),
        "in_wself": np.ascontiguousarray(L1_gnn_self_weight), "in_bias": np.asarray(L1_gnn_bias).reshape(1, P),
    }
    nc = bacc.Bacc("TRN2", target_bir_lowering=False, num_devices=1)
    args = [nc.dram_tensor(n, a.shape, mybir.dt.from_np(a.dtype), kind="ExternalInput").ap() for n, a in arrays.items()]
    args.append(nc.dram_tensor("out_x", arrays["in_x"].shape, F32, kind="ExternalOutput").ap())
    gnn_kernel(nc, *args)
    return run_bass_kernel_spmd(nc, [arrays], core_ids=[0]).results[0]["out_x"]
```
